# Optimizing a Trainium2 kernel written in Bass

```python
import numpy as np
import jax
import jax.numpy as jnp

def _softmax(x, axis=-1):
    return jax.nn.softmax(x, axis=axis)

def _gelu(x):
    return jax.nn.gelu(x, approximate=True)

def _silu(x):
    return jax.nn.silu(x)

def _sigmoid(x):
    return jax.nn.sigmoid(x)

def _layernorm(x, axis=-1, eps=1e-05):
    m = jnp.mean(x, axis=axis, keepdims=True)
    v = jnp.var(x, axis=axis, keepdims=True)
    return (x - m) / jnp.sqrt(v + eps)

def _scatter_add(tgt, idx, src, axis=0):
    return tgt.at[idx].add(src)

def _segment_sum(src, seg, n):
    return jax.ops.segment_sum(src, seg, n)
kernel_name = 'mk_dlrm_tower_d1_rec_r8_55f27a'

def setup_inputs(seed: int=0):
    np.random.seed(seed)
    _w = jnp.asarray

    def _rec_inputs():
        import jax
        import jax.numpy as jnp
        _tk = jax.random.key(seed)
        ids = jnp.stack([jax.random.randint(jax.random.fold_in(_tk, 200 + f), (2048,), 0, v, jnp.int32) for f, v in enumerate([1000, 1000, 12500, 1000, 1250, 125000, 1250, 12500, 1000, 1250, 12500, 1000, 12500, 1000, 1250, 1000, 1250, 12500, 1000, 12500, 1000, 1250, 12500, 1250, 1000, 1000])], axis=1)
        tbl_0 = 0.05 * jax.random.normal(jax.random.fold_in(_tk, 500 + 0), (1000, 128), jnp.float32)
        tbl_1 = 0.05 * jax.random.normal(jax.random.fold_in(_tk, 500 + 1), (1000, 128), jnp.float32)
        tbl_2 = 0.05 * jax.random.normal(jax.random.fold_in(_tk, 500 + 2), (12500, 128), jnp.float32)
        tbl_3 = 0.05 * jax.random.normal(jax.random.fold_in(_tk, 500 + 3), (1000, 128), jnp.float32)
        tbl_4 = 0.05 * jax.random.normal(jax.random.fold_in(_tk, 500 + 4), (1250, 128), jnp.float32)
        tbl_5 = 0.05 * jax.random.normal(jax.random.fold_in(_tk, 500 + 5), (125000, 128), jnp.float32)
        tbl_6 = 0.05 * jax.random.normal(jax.random.fold_in(_tk, 500 + 6), (1250, 128), jnp.float32)
        tbl_7 = 0.05 * jax.random.normal(jax.random.fold_in(_tk, 500 + 7), (12500, 128), jnp.float32)
        tbl_8 = 0.05 * jax.random.normal(jax.random.fold_in(_tk, 500 + 8), (1000, 128), jnp.float32)
        tbl_9 = 0.05 * jax.random.normal(jax.random.fold_in(_tk, 500 + 9), (1250, 128), jnp.float32)
        tbl_10 = 0.05 * jax.random.normal(jax.random.fold_in(_tk, 500 + 10), (12500, 128), jnp.float32)
        tbl_11 = 0.05 * jax.random.normal(jax.random.fold_in(_tk, 500 + 11), (1000, 128), jnp.float32)
        tbl_12 = 0.05 * jax.random.normal(jax.random.fold_in(_tk, 500 + 12), (12500, 128), jnp.float32)
        tbl_13 = 0.05 * jax.random.normal(jax.random.fold_in(_tk, 500 + 13), (1000, 128), jnp.float32)
        tbl_14 = 0.05 * jax.random.normal(jax.random.fold_in(_tk, 500 + 14), (1250, 128), jnp.float32)
        tbl_15 = 0.05 * jax.random.normal(jax.random.fold_in(_tk, 500 + 15), (1000, 128), jnp.float32)
        tbl_16 = 0.05 * jax.random.normal(jax.random.fold_in(_tk, 500 + 16), (1250, 128), jnp.float32)
        tbl_17 = 0.05 * jax.random.normal(jax.random.fold_in(_tk, 500 + 17), (12500, 128), jnp.float32)
        tbl_18 = 0.05 * jax.random.normal(jax.random.fold_in(_tk, 500 + 18), (1000, 128), jnp.float32)
        tbl_19 = 0.05 * jax.random.normal(jax.random.fold_in(_tk, 500 + 19), (12500, 128), jnp.float32)
        tbl_20 = 0.05 * jax.random.normal(jax.random.fold_in(_tk, 500 + 20), (1000, 128), jnp.float32)
        tbl_21 = 0.05 * jax.random.normal(jax.random.fold_in(_tk, 500 + 21), (1250, 128), jnp.float32)
        tbl_22 = 0.05 * jax.random.normal(jax.random.fold_in(_tk, 500 + 22), (12500, 128), jnp.float32)
        tbl_23 = 0.05 * jax.random.normal(jax.random.fold_in(_tk, 500 + 23), (1250, 128), jnp.float32)
        tbl_24 = 0.05 * jax.random.normal(jax.random.fold_in(_tk, 500 + 24), (1000, 128), jnp.float32)
        tbl_25 = 0.05 * jax.random.normal(jax.random.fold_in(_tk, 500 + 25), (1000, 128), jnp.float32)
        _rk = jax.random.fold_in(_tk, 7)
        r_dense_proj = -0.000520686 + 1.00062 * jax.random.normal(jax.random.fold_in(_rk, 101), (2048, 128), jnp.float32)
        W_top1 = 0.0405887 * jax.random.normal(jax.random.fold_in(_tk, 801), (607, 512), jnp.float32)
        W_top2 = 0.0441942 * jax.random.normal(jax.random.fold_in(_tk, 802), (512, 256), jnp.float32)
        W_top3 = 0.0625 * jax.random.normal(jax.random.fold_in(_tk, 803), (256, 1), jnp.float32)
        b_top1 = jnp.zeros((512,), jnp.float32)
        b_top2 = jnp.zeros((256,), jnp.float32)
        return (r_dense_proj, ids, tbl_0, tbl_1, tbl_2, tbl_3, tbl_4, tbl_5, tbl_6, tbl_7, tbl_8, tbl_9, tbl_10, tbl_11, tbl_12, tbl_13, tbl_14, tbl_15, tbl_16, tbl_17, tbl_18, tbl_19, tbl_20, tbl_21, tbl_22, tbl_23, tbl_24, tbl_25, W_top1, b_top1, W_top2, b_top2, W_top3)
    r_dense_proj, ids, tbl_0, tbl_1, tbl_2, tbl_3, tbl_4, tbl_5, tbl_6, tbl_7, tbl_8, tbl_9, tbl_10, tbl_11, tbl_12, tbl_13, tbl_14, tbl_15, tbl_16, tbl_17, tbl_18, tbl_19, tbl_20, tbl_21, tbl_22, tbl_23, tbl_24, tbl_25, W_top1, b_top1, W_top2, b_top2, W_top3 = _rec_inputs()

    def _L0_rec_setup():
        import jax, jax.numpy as jnp
        import numpy as np
        key = jax.random.key(seed)
        k1, k2 = jax.random.split(key)
        B, N_SPARSE, D = (2048, 26, 128)
        dense_proj = jax.random.normal(k1, (B, D), dtype=jnp.float32)
        sparse_embs = jax.random.normal(k2, (B, N_SPARSE, D), dtype=jnp.float32)
        return {'dense_proj': dense_proj, 'sparse_embs': sparse_embs}
    _L0_rec_all = _L0_rec_setup()
    _L0_rec_in = {k: v for k, v in _L0_rec_all.items() if k in ()}
    del _L0_rec_all
    return {'r_dense_proj': r_dense_proj, 'ids': ids, 'tbl_0': tbl_0, 'tbl_1': tbl_1, 'tbl_2': tbl_2, 'tbl_3': tbl_3, 'tbl_4': tbl_4, 'tbl_5': tbl_5, 'tbl_6': tbl_6, 'tbl_7': tbl_7, 'tbl_8': tbl_8, 'tbl_9': tbl_9, 'tbl_10': tbl_10, 'tbl_11': tbl_11, 'tbl_12': tbl_12, 'tbl_13': tbl_13, 'tbl_14': tbl_14, 'tbl_15': tbl_15, 'tbl_16': tbl_16, 'tbl_17': tbl_17, 'tbl_18': tbl_18, 'tbl_19': tbl_19, 'tbl_20': tbl_20, 'tbl_21': tbl_21, 'tbl_22': tbl_22, 'tbl_23': tbl_23, 'tbl_24': tbl_24, 'tbl_25': tbl_25, 'W_top1': W_top1, 'b_top1': b_top1, 'W_top2': W_top2, 'b_top2': b_top2, 'W_top3': W_top3}

def reference(r_dense_proj, ids, tbl_0, tbl_1, tbl_2, tbl_3, tbl_4, tbl_5, tbl_6, tbl_7, tbl_8, tbl_9, tbl_10, tbl_11, tbl_12, tbl_13, tbl_14, tbl_15, tbl_16, tbl_17, tbl_18, tbl_19, tbl_20, tbl_21, tbl_22, tbl_23, tbl_24, tbl_25, W_top1, b_top1, W_top2, b_top2, W_top3):
    import jax
    import jax.numpy as jnp

    def _L0_rec_ref(dense_proj, sparse_embs):
        import jax, jax.numpy as jnp
        import numpy as np
        all_vecs = jnp.concatenate([dense_proj[:, None, :], sparse_embs], axis=1)
        n = all_vecs.shape[1]
        interactions = jnp.einsum('bnd,bmd->bnm', all_vecs, all_vecs)
        rows, cols = np.triu_indices(n, k=1)
        interact_flat = interactions[:, rows, cols]
        return jnp.concatenate([dense_proj, interact_flat], axis=1)
    e = jnp.stack([tbl_0[ids[:, 0]], tbl_1[ids[:, 1]], tbl_2[ids[:, 2]], tbl_3[ids[:, 3]], tbl_4[ids[:, 4]], tbl_5[ids[:, 5]], tbl_6[ids[:, 6]], tbl_7[ids[:, 7]], tbl_8[ids[:, 8]], tbl_9[ids[:, 9]], tbl_10[ids[:, 10]], tbl_11[ids[:, 11]], tbl_12[ids[:, 12]], tbl_13[ids[:, 13]], tbl_14[ids[:, 14]], tbl_15[ids[:, 15]], tbl_16[ids[:, 16]], tbl_17[ids[:, 17]], tbl_18[ids[:, 18]], tbl_19[ids[:, 19]], tbl_20[ids[:, 20]], tbl_21[ids[:, 21]], tbl_22[ids[:, 22]], tbl_23[ids[:, 23]], tbl_24[ids[:, 24]], tbl_25[ids[:, 25]]], axis=1)
    z = _L0_rec_ref(r_dense_proj, e)
    z = z.reshape(z.shape[0], -1)
    h = jnp.concatenate([z, r_dense_proj], axis=1)
    h = jnp.maximum(h @ W_top1 + b_top1, 0.0)
    h = jnp.maximum(h @ W_top2 + b_top2, 0.0)
    y = h @ W_top3
    return y

_drawn_inputs = setup_inputs


def setup_inputs(seed=0):
    import zlib

    import numpy as np

    out = dict(_drawn_inputs(seed))
    spreads = {'b_top1': (0.0, 0.1), 'b_top2': (0.0, 0.1)}
    factors = {}
    for name, (base, spread) in spreads.items():
        noise = np.random.default_rng([zlib.crc32(name.encode()), seed]).standard_normal(out[name].shape)
        drawn = base * np.exp(spread * noise) if base else spread * noise
        out[name] = jnp.asarray(drawn.astype(out[name].dtype))
    for name, factor in factors.items():
        out[name] = (out[name] * factor).astype(out[name].dtype)
    return out
```

```python
from contextlib import ExitStack

import numpy as np

import concourse.bass as bass
from concourse import mybir

F32 = mybir.dt.float32
I32 = mybir.dt.int32
ACT = mybir.ActivationFunctionType
ALU = mybir.AluOpType

P = 128
D = 128
TABLES = 26
VECS = TABLES + 1
ROW = 28
HALF = ROW // 2
FOLD = HALF - 1
QUAD = 32
PAIRS = VECS * (VECS - 1) // 2
CHUNKS = 3
CHUNK = PAIRS // CHUNKS
GROUP = 4
GROUPS = -(-VECS // GROUP)
DVE_GROUPS = (0, 2, 4, 6)
ACT_GROUPS = (1, 3, 5)
H1, H2 = 512, 256


def pair_rows():
    rows = []
    for i in range(FOLD):
        for p in range(VECS):
            a, b = (p, i + HALF) if p < i + HALF else (i, p - FOLD)
            rows.append(a * VECS - a * (a + 1) // 2 + b - a - 1)
    return np.array(rows)


def build(nc, dense, ids, tables, w1_dense, w1_pairs, b1, w2, b2, w3, fold_mask, identity, out):
    batch = dense.shape[0]
    tiles = batch // P
    assert tiles % 2 == 0 and tiles >= 4

    with ExitStack() as ctx:
        def sb(name, shape, dt=F32):
            return ctx.enter_context(nc.sbuf_tensor(name, shape, dt))

        def psum(name, shape):
            return ctx.enter_context(nc.psum_tensor(name, shape, F32))

        def sem(name):
            return ctx.enter_context(nc.semaphore(name))

        ids_sb = [sb(f"ids{j}", [P, TABLES], I32) for j in range(2)]
        vecs = [sb(f"vecs{j}", [P, VECS, D]) for j in range(2)]
        vecs_T = sb("vecs_T", [D, P, ROW])
        dense_T = [sb(f"dense_T{j}", [D, P]) for j in range(2)]
        gram_rows = sb("gram_rows", [P, 2, FOLD, QUAD])
        pair_rows_sb = sb("pair_rows_sb", [P, PAIRS])
        pairs_T = sb("pairs_T", [P, CHUNKS, P])
        h1_T = sb("h1_T", [P, H1 // P, P])
        h2_T = sb("h2_T", [P, H2 // P, P])
        y_row = sb("y_row", [1, batch])
        w1d = sb("w1d", [D, 2, H1])
        w1p = sb("w1p", [P, CHUNKS, H1])
        w2_sb = sb("w2_sb", [P, H1 // P, H2])
        b2_sb = sb("b2_sb", [P, H2 // P])
        w3_sb = sb("w3_sb", [P, H2 // P])
        ident = sb("ident", [P, P])
        mask = sb("mask", [P, FOLD, FOLD], I32)

        vec_dve = [psum(f"vec_dve{j}", [P, GROUP, P]) for j in range(2)]
        vec_act = [psum(f"vec_act{j}", [P, GROUP, P]) for j in range(2)]
        gram = psum("gram", [P, QUAD, QUAD])
        small = psum("small", [P, 512])
        hid1 = psum("hid1", [P, H1 // P, P])
        pairs_ps = small[:, 0:CHUNKS * P].rearrange("p (c b) -> p c b", c=CHUNKS)
        hid2 = small[:, 0:H2].rearrange("p (c b) -> p c b", c=H2 // P)
        y_ps = small[0:1, CHUNKS * P:CHUNKS * P + P]

        ids_in = [sem(f"ids_in{j}") for j in range(2)]
        dense_in = [sem(f"dense_in{j}") for j in range(2)]
        gathered = [sem(f"gathered{j}") for j in range(2)]
        gather_begun, fold_begun = sem("gather_begun"), sem("fold_begun")
        ident_in, weights_in, mask_in = sem("ident_in"), sem("weights_in"), sem("mask_in")
        dve_set, w1d_summed = sem("dve_set"), sem("w1d_summed")
        turned_dve, turned_act = sem("turned_dve"), sem("turned_act")
        copied_dve, copied_act = sem("copied_dve"), sem("copied_act")
        gram_ready, gram_turned = sem("gram_ready"), sem("gram_turned")
        half_copied, folded = sem("half_copied"), sem("folded")
        pairs_ready, pairs_copied = sem("pairs_ready"), sem("pairs_copied")
        h1_ready, h1_copied = sem("h1_ready"), sem("h1_copied")
        h2_ready, h2_copied = sem("h2_ready"), sem("h2_copied")
        y_ready, y_copied, y_out = sem("y_ready"), sem("y_copied"), sem("y_out")

        def at(n):
            return bass.ds(n * P, P)

        with nc.Block() as block:

            @block.sync
            def _(sp):
                def load(t, j, first):
                    if not first:
                        sp.wait_ge(turned_dve, 4 * (t - 1))
                    sp.dma_start(ids_sb[j][:, :], ids[at(t), :]).then_inc(ids_in[j], 16)
                    sp.dma_start(vecs[j][:, 0, :], dense[at(t), :]).then_inc(dense_in[j], 16)

                load(0, 0, True)
                load(1, 1, True)
                sp.dma_start(ident[:, :], identity).then_inc(ident_in, 16)
                sp.dma_start(mask[:, :, :].rearrange("p i q -> p (i q)"), fold_mask).then_inc(mask_in, 16)
                sp.dma_start(w1d[:, :, :], w1_dense.rearrange("(c k) n -> k c n", k=D)).then_inc(weights_in, 16)
                sp.dma_start(w1p[0:CHUNK, :, :], w1_pairs.rearrange("(c k) n -> k c n", k=CHUNK)).then_inc(weights_in, 16)
                sp.dma_start(w1p[CHUNK:CHUNK + 1, 0, :], b1).then_inc(weights_in, 16)
                sp.dma_start(w2_sb[:, :, :], w2.rearrange("(c k) n -> k c n", k=P)).then_inc(weights_in, 16)
                sp.dma_start(b2_sb[:, :], b2).then_inc(weights_in, 16)
                sp.dma_start(w3_sb[:, :], w3).then_inc(weights_in, 16)
                with sp.Fori(1, tiles // 2) as r:
                    load(2 * r, 0, False)
                    load(2 * r + 1, 1, False)
                sp.wait_ge(y_copied, tiles)
                sp.dma_start(out, y_row[0:1, :]).then_inc(y_out, 16)
                sp.wait_ge(y_out, 16)

            @block.gpsimd
            def _(pool):
                def gather(t, j, n, first):
                    if not first:
                        pool.wait_ge(turned_dve, 4 * (t - 1))
                    pool.wait_ge(ids_in[j], 16 * n)
                    pool.sem_inc(gather_begun, 1)
                    for k in range(TABLES):
                        nc.gpsimd.indirect_dma_start(
                            out=vecs[j][:, 1 + k, :], out_offset=None, in_=tables[k],
                            in_offset=bass.IndirectOffsetOnAxis(ap=ids_sb[j][:, k:k + 1], axis=0),
                        ).then_inc(gathered[j], 16)

                gather(0, 0, 1, True)
                gather(1, 1, 1, True)
                with pool.Fori(1, tiles // 2) as r:
                    gather(2 * r, 0, r + 1, False)
                    gather(2 * r + 1, 1, r + 1, False)

            @block.tensor
            def _(pe):
                def turn_group(t, j, q):
                    if q in DVE_GROUPS:
                        k = DVE_GROUPS.index(q)
                        n = 4 * t + k
                        bank, ready, copied = vec_dve[k % 2], turned_dve, copied_dve
                    else:
                        k = ACT_GROUPS.index(q)
                        n = 3 * t + k
                        bank, ready, copied = vec_act[(3 * j + k) % 2], turned_act, copied_act
                    if not (isinstance(n, int) and n < 2):
                        pe.wait_ge(copied, n - 1)
                    members = range(q * GROUP, min(VECS, (q + 1) * GROUP))
                    for v in members:
                        last = nc.tensor.transpose(bank[:, v - q * GROUP, :], vecs[j][:, v, :], ident[:, :])
                    last.then_inc(ready, 1)
                    return last

                def pairs_out(t):
                    pe.wait_ge(folded, t + 1)
                    if not (isinstance(t, int) and t < 1):
                        pe.wait_ge(y_copied, t)
                    for c in range(CHUNKS):
                        last = nc.tensor.transpose(
                            pairs_ps[0:CHUNK, c, :],
                            pair_rows_sb[:, c * CHUNK:(c + 1) * CHUNK], ident[:, :])
                    last.then_inc(pairs_ready, 1)

                def layer1(t, j):
                    pe.wait_ge(pairs_copied, t + 1)
                    if not (isinstance(t, int) and t < 1):
                        pe.wait_ge(h1_copied, t)
                    for o in range(H1 // P):
                        cols = slice(o * P, (o + 1) * P)
                        nc.tensor.matmul(hid1[:, o, :], w1d[:, 0, cols], dense_T[j][:, :], start=True, stop=False)
                        for c in range(CHUNKS):
                            k = CHUNK + 1 if c == 0 else CHUNK
                            last = nc.tensor.matmul(hid1[:, o, :], w1p[0:k, c, cols], pairs_T[0:k, c, :],
                                                    start=False, stop=c == CHUNKS - 1)
                    last.then_inc(h1_ready, 1)

                def layer2(t):
                    pe.wait_ge(h1_copied, t + 1)
                    for o in range(H2 // P):
                        for c in range(H1 // P):
                            last = nc.tensor.matmul(hid2[:, o, :], w2_sb[:, c, o * P:(o + 1) * P], h1_T[:, c, :],
                                                    start=c == 0, stop=c == H1 // P - 1)
                    last.then_inc(h2_ready, 1)

                def layer3(t):
                    pe.wait_ge(h2_copied, t + 1)
                    for c in range(H2 // P):
                        last = nc.tensor.matmul(y_ps, w3_sb[:, c:c + 1], h2_T[:, c, :],
                                                start=c == 0, stop=c == H2 // P - 1)
                    last.then_inc(y_ready, 1)

                def gram_part(lo, hi):
                    for g in range(lo, hi):
                        for s in range(P // QUAD):
                            b = s * QUAD + g
                            v = vecs_T[:, b, :]
                            last = nc.tensor.matmul(
                                gram[s * QUAD:s * QUAD + VECS, g, 0:2 * FOLD], v[:, 0:VECS],
                                v.rearrange("d (h n) -> d h n", h=2)[:, :, 0:FOLD], start=True, stop=True)
                    return last

                def tile(t, j, n, first=False, begin=None):
                    pe.wait_ge(dense_in[j], 16 * n)
                    pe.wait_ge(gathered[j], 16 * TABLES * n)
                    turn_group(t, j, 0)
                    turn_group(t, j, 1)
                    turn_group(t, j, 2)
                    if not first:
                        pairs_out(t - 1)
                    turn_group(t, j, 3)
                    if not first:
                        layer1(t - 1, 1 - j)
                    turn_group(t, j, 4)
                    turn_group(t, j, 5)
                    turn_group(t, j, 6)
                    if not first:
                        layer2(t - 1)
                    pe.wait_ge(copied_dve, 4 * t + 4)
                    pe.wait_ge(copied_act, 3 * t + 3)
                    if not first:
                        pe.wait_ge(gram_turned, t)
                    gram_part(0, 8)
                    if not first:
                        layer3(t - 1)
                    gram_part(8, QUAD).then_inc(gram_ready, 1)

                pe.wait_ge(ident_in, 16)
                pe.wait_ge(dve_set, 3)
                tile(0, 0, 1, first=True)
                pe.wait_ge(weights_in, 6 * 16)
                pe.wait_ge(w1d_summed, 1)
                tile(1, 1, 1)
                with pe.Fori(1, tiles // 2) as r:
                    tile(2 * r, 0, r + 1)
                    tile(2 * r + 1, 1, r + 1)
                end = tiles - 1
                pairs_out(end)
                layer1(end, end % 2)
                layer2(end)
                layer3(end)

            def copy_group(engine_copy, bank, q):
                lo, hi = q * GROUP, min(VECS, (q + 1) * GROUP)
                return engine_copy(vecs_T[:, :, lo:hi].rearrange("d b v -> d v b"), bank[:, 0:hi - lo, :])

            @block.vector
            def _(dve):
                def turn(t, first=False):
                    dve.wait_ge(gram_ready, t + 1)
                    nc.vector.transpose(gram_rows[:, :, :, :].rearrange("p h n m -> p (h n m)"),
                                        gram[:, :, 0:2 * FOLD].rearrange("p g n -> p n g")).then_inc(gram_turned, 1)
                    block_ip = pair_rows_sb[:, :].rearrange("p (i m) -> p i m", i=FOLD)
                    dve.wait_ge(gram_turned, t + 1)
                    if not first:
                        dve.wait_ge(pairs_ready, t)
                    nc.vector.tensor_copy(block_ip, gram_rows[:, 1, :, 0:VECS]).then_inc(half_copied, 1)
                    dve.wait_ge(half_copied, t + 1)
                    dve.sem_inc(fold_begun, 1)
                    nc.vector.copy_predicated(block_ip[:, :, HALF:VECS], mask[:, :, :],
                                              gram_rows[:, 0, :, 1:HALF]).then_inc(folded, 1)

                def copies(t, j):
                    for k, q in enumerate(DVE_GROUPS):
                        dve.wait_ge(turned_dve, 4 * t + k + 1)
                        if q == 0:
                            nc.vector.tensor_copy(dense_T[j][:, :], vec_dve[0][:, 0, :])
                        copy_group(nc.vector.tensor_copy, vec_dve[k % 2], q).then_inc(copied_dve, 1)

                nc.vector.memset(gram[:, 0:16, :], 0.0).then_inc(dve_set, 1)
                nc.vector.memset(gram[:, 16:32, :], 0.0).then_inc(dve_set, 1)
                nc.vector.memset(pairs_T[96:P, :, :], 1.0).then_inc(dve_set, 1)
                copies(0, 0)
                dve.wait_ge(mask_in, 16)
                dve.wait_ge(weights_in, 6 * 16)
                nc.vector.tensor_tensor(w1d[:, 0, :], w1d[:, 0, :], w1d[:, 1, :], ALU.add).then_inc(w1d_summed, 1)
                turn(0, first=True)
                copies(1, 1)
                with dve.Fori(1, tiles // 2) as r:
                    turn(2 * r - 1)
                    copies(2 * r, 0)
                    turn(2 * r)
                    copies(2 * r + 1, 1)
                turn(tiles - 1)

            @block.scalar
            def _(act):
                def copy(t, j, k):
                    act.wait_ge(turned_act, 3 * t + k + 1)
                    copy_group(nc.scalar.copy, vec_act[(3 * j + k) % 2], ACT_GROUPS[k]).then_inc(copied_act, 1)

                def pairs(t):
                    act.wait_ge(pairs_ready, t + 1)
                    nc.scalar.copy(pairs_T[0:CHUNK, :, :], pairs_ps[0:CHUNK, :, :]).then_inc(pairs_copied, 1)

                def relu1(t):
                    act.wait_ge(h1_ready, t + 1)
                    nc.scalar.activation(h1_T[:, :, :], hid1[:, :, :], ACT.Relu).then_inc(h1_copied, 1)

                def relu2(t):
                    act.wait_ge(h2_ready, t + 1)
                    nc.scalar.activation(h2_T[:, 0, :], hid2[:, 0, :], ACT.Relu, bias=b2_sb[:, 0:1])
                    nc.scalar.activation(h2_T[:, 1, :], hid2[:, 1, :], ACT.Relu,
                                         bias=b2_sb[:, 1:2]).then_inc(h2_copied, 1)

                def result(t):
                    act.wait_ge(y_ready, t + 1)
                    nc.scalar.copy(y_row[0:1, at(t)], y_ps).then_inc(y_copied, 1)

                def tile(t, j):
                    copy(t, j, 0)
                    pairs(t - 1)
                    copy(t, j, 1)
                    relu1(t - 1)
                    copy(t, j, 2)
                    relu2(t - 1)
                    result(t - 1)

                for k in range(3):
                    copy(0, 0, k)
                act.wait_ge(dve_set, 3)
                act.wait_ge(weights_in, 6 * 16)
                tile(1, 1)
                with act.Fori(1, tiles // 2) as r:
                    tile(2 * r, 0)
                    tile(2 * r + 1, 1)
                end = tiles - 1
                pairs(end)
                relu1(end)
                relu2(end)
                result(end)


def kernel(**inputs):
    import concourse.bacc as bacc
    from concourse.bass_utils import run_bass_kernel_spmd

    nc = bacc.Bacc("TRN2", target_bir_lowering=False, num_devices=1)
    w1 = np.asarray(inputs["W_top1"])
    dense = np.ascontiguousarray(inputs["r_dense_proj"])
    arrays = {
        "dense": dense,
        "ids": np.ascontiguousarray(inputs["ids"]),
        "w1_dense": np.ascontiguousarray(np.concatenate([w1[0:D], w1[D + PAIRS:]], axis=0)),
        "w1_pairs": np.ascontiguousarray(w1[D:D + PAIRS][pair_rows()]),
        "b1": np.ascontiguousarray(np.asarray(inputs["b_top1"]).reshape(1, H1)),
        "w2": np.ascontiguousarray(inputs["W_top2"]),
        "b2": np.ascontiguousarray(np.asarray(inputs["b_top2"]).reshape(H2 // P, P).T),
        "w3": np.ascontiguousarray(np.asarray(inputs["W_top3"]).reshape(H2 // P, P).T),
        "fold_mask": np.ascontiguousarray(np.broadcast_to(
            np.triu(np.ones((FOLD, FOLD), np.int32)).reshape(1, -1), (P, FOLD * FOLD))),
        "identity": np.eye(P, dtype=np.float32),
    }
    for k in range(TABLES):
        arrays[f"tbl_{k}"] = np.ascontiguousarray(inputs[f"tbl_{k}"])
    ap = {name: nc.dram_tensor(name, a.shape, mybir.dt.from_np(a.dtype), kind="ExternalInput").ap()
          for name, a in arrays.items()}
    out = nc.dram_tensor("y", (1, dense.shape[0]), F32, kind="ExternalOutput").ap()
    build(nc, ap["dense"], ap["ids"], [ap[f"tbl_{k}"] for k in range(TABLES)], ap["w1_dense"], ap["w1_pairs"],
          ap["b1"], ap["w2"], ap["b2"], ap["w3"], ap["fold_mask"], ap["identity"], out)
    r = run_bass_kernel_spmd(nc, [arrays], core_ids=[0])
    return r.results[0]["y"].reshape(dense.shape[0], 1)
```

```python
from contextlib import ExitStack

import numpy as np

import concourse.bass as bass
from concourse import mybir

F32 = mybir.dt.float32
F32R = mybir.dt.float32r
I32 = mybir.dt.int32
ACT = mybir.ActivationFunctionType
ALU = mybir.AluOpType

P = 128
D = 128
TABLES = 26
VECS = TABLES + 1
LOOKUPS = 7
LOOK_ROWS = 1000
LOOK_K = 125
LOOK_CH = LOOK_ROWS // LOOK_K
UNIT_CH = LOOK_CH // 2
GATHERS = TABLES - LOOKUPS
ROWS = 1 + GATHERS
ROW = 28
HALF = ROW // 2
FOLD = HALF - 1
QUAD = 32
PAIRS = VECS * (VECS - 1) // 2
CHUNKS = 3
CHUNK = PAIRS // CHUNKS
GROUP = 4
GROUPS = -(-ROWS // GROUP)
DVE_GROUPS = (1, 3)
ACT_GROUPS = (0, 2, 4)
GRAM_PARTS = (0, 6, 11, 16, 21, 26, 32)
H1, H2 = 512, 256


def pair_rows(fields):
    vector = [0] + [1 + f for f in fields]
    rows = []
    for i in range(FOLD):
        for p in range(VECS):
            a, b = (p, i + HALF) if p < i + HALF else (i, p - FOLD)
            a, b = sorted((vector[a], vector[b]))
            rows.append(a * VECS - a * (a + 1) // 2 + b - a - 1)
    return np.array(rows)


def build(nc, dense, ids, look_ids, tables, look_tables, w1_dense, w1_pairs, b1, w2, b2, w3,
          fold_mask, identity, row_numbers, out):
    batch = dense.shape[0]
    tiles = batch // P
    pairs = tiles // 2
    assert tiles % 2 == 0 and pairs >= 3 and len(tables) == GATHERS and GROUPS == 5
    PAIR = 2 * P

    with ExitStack() as ctx:
        def sb(name, shape, dt=F32):
            return ctx.enter_context(nc.sbuf_tensor(name, shape, dt))

        def psum(name, shape):
            return ctx.enter_context(nc.psum_tensor(name, shape, F32))

        def sem(name):
            return ctx.enter_context(nc.semaphore(name))

        ids_sb = [sb(f"ids{j}", [P, GATHERS], I32) for j in range(2)]
        vecs = [sb(f"vecs{j}", [P, ROWS, D]) for j in range(2)]
        vecs_T = [sb(f"vecs_T{j}", [D, P, ROW]) for j in range(2)]
        dense_T = [sb(f"dense_T{j}", [D, P]) for j in range(2)]
        look_raw = [sb(f"look_raw{k}", [LOOK_K, LOOK_CH * D]) for k in range(2)]
        look_hi = sb("look_hi", [LOOK_K, LOOKUPS, LOOK_CH, D], F32R)
        look_lo = sb("look_lo", [LOOK_K, LOOKUPS, LOOK_CH, D], F32R)
        STEP_IDS = -(-LOOKUPS // 2)
        step_ids = [sb(f"step_ids{a}", [P, STEP_IDS, PAIR], I32) for a in range(2)]
        onehot = sb("onehot", [LOOK_K, LOOKUPS, UNIT_CH, PAIR], F32R)
        looked = sb("looked", [D, LOOKUPS, PAIR])
        row_no = sb("row_no", [P, LOOK_CH])
        gram_rows = sb("gram_rows", [P, 2, FOLD, QUAD])
        pair_rows_sb = sb("pair_rows_sb", [P, PAIRS])
        pairs_T = sb("pairs_T", [P, CHUNKS, P])
        h1_T = sb("h1_T", [P, H1 // P, P])
        h2_T = sb("h2_T", [P, H2 // P, P])
        y_row = sb("y_row", [1, batch])
        w1d = sb("w1d", [D, 2, H1])
        w1p = sb("w1p", [P, CHUNKS, H1])
        w2_sb = sb("w2_sb", [P, H1 // P, H2])
        b2_sb = sb("b2_sb", [P, H2 // P])
        w3_sb = sb("w3_sb", [P, H2 // P])
        ident = sb("ident", [P, P])
        mask = sb("mask", [P, FOLD, FOLD], I32)

        vec_dve = psum("vec_dve", [P, GROUP, P])
        vec_act = [psum(f"vec_act{j}", [P, GROUP, P]) for j in range(2)]
        gram = psum("gram", [P, QUAD, QUAD])
        small = psum("small", [P, 512])
        hid1 = psum("hid1", [P, H1 // P, P])
        look_ps = psum("look_ps", [D, 512])[:, 0:PAIR]
        pairs_ps = small[:, 0:CHUNKS * P].rearrange("p (c b) -> p c b", c=CHUNKS)
        hid2 = small[:, 0:H2].rearrange("p (c b) -> p c b", c=H2 // P)
        y_ps = small[0:1, CHUNKS * P:CHUNKS * P + P]

        ids_in = [sem(f"ids_in{j}") for j in range(2)]
        dense_in = [sem(f"dense_in{j}") for j in range(2)]
        gathered = [sem(f"gathered{j}") for j in range(2)]
        step_ids_in = [sem(f"step_ids_in{a}") for a in range(2)]
        table_in = [sem(f"table_in{k}") for k in range(LOOKUPS)]
        table_high, table_split = sem("table_high"), sem("table_split")
        onehot_made, onehot_used, looked_up, merged = sem("onehot_made"), sem("onehot_used"), sem("looked_up"), sem("merged")
        gather_begun, fold_begun = sem("gather_begun"), sem("fold_begun")
        ident_in, weights_in, mask_in, row_no_in = sem("ident_in"), sem("weights_in"), sem("mask_in"), sem("row_no_in")
        dve_set, w1d_summed = sem("dve_set"), sem("w1d_summed")
        turned_dve, turned_act = sem("turned_dve"), sem("turned_act")
        copied_dve, copied_act, dense_copied = sem("copied_dve"), sem("copied_act"), sem("dense_copied")
        gram_ready, gram_turned = sem("gram_ready"), sem("gram_turned")
        half_copied, folded = sem("half_copied"), sem("folded")
        pairs_ready, pairs_copied = sem("pairs_ready"), sem("pairs_copied")
        h1_ready, h1_copied = sem("h1_ready"), sem("h1_copied")
        h2_ready, h2_copied = sem("h2_ready"), sem("h2_copied")
        y_ready, y_copied, y_out = sem("y_ready"), sem("y_copied"), sem("y_out")

        def at(n):
            return bass.ds(n * P, P)

        def positive(n):
            return not isinstance(n, int) or n > 0

        def units(a):
            return [(i, (a * LOOKUPS + i) // 2, (a * LOOKUPS + i) % 2) for i in range(LOOKUPS)]

        with nc.Block() as block:

            @block.sync
            def _(sp):
                def load(t, j):
                    if positive(t - 1):
                        sp.wait_ge(turned_act, len(ACT_GROUPS) * (t - 1))
                    sp.dma_start(ids_sb[j][:, :], ids[at(t), :]).then_inc(ids_in[j], 16)
                    sp.dma_start(vecs[j][:, 0, :], dense[at(t), :]).then_inc(dense_in[j], 16)

                def load_step(s, a, pair):
                    if positive(s - 1):
                        sp.wait_ge(onehot_made, LOOKUPS * (s - 1))
                    first = a * LOOKUPS // 2
                    src = look_ids[first:first + STEP_IDS, bass.ds(pair * PAIR, PAIR)]
                    sp.dma_start(step_ids[a][:, :, :],
                                 src.unsqueeze(0).broadcast_to([P, STEP_IDS, PAIR])).then_inc(step_ids_in[a], 16)

                load(0, 0)
                sp.dma_start(row_no[:, :], row_numbers).then_inc(row_no_in, 16)
                load_step(0, 0, 0)
                load_step(1, 1, 0)
                load(1, 1)
                sp.dma_start(ident[:, :], identity).then_inc(ident_in, 16)
                for k in range(LOOKUPS):
                    if k >= 2:
                        sp.wait_ge(table_split, k - 1)
                    sp.dma_start(look_raw[k % 2][:, :], look_tables[k].rearrange("(p c) d -> p (c d)", c=LOOK_CH)
                                 ).then_inc(table_in[k], 16)
                sp.dma_start(mask[:, :, :].rearrange("p i q -> p (i q)"), fold_mask).then_inc(mask_in, 16)
                sp.dma_start(w1d[:, :, :], w1_dense.rearrange("(c k) n -> k c n", k=D)).then_inc(weights_in, 16)
                sp.dma_start(w1p[0:CHUNK, :, :], w1_pairs.rearrange("(c k) n -> k c n", k=CHUNK)).then_inc(weights_in, 16)
                sp.dma_start(w1p[CHUNK:CHUNK + 1, 0, :], b1).then_inc(weights_in, 16)
                sp.dma_start(w2_sb[:, :, :], w2.rearrange("(c k) n -> k c n", k=P)).then_inc(weights_in, 16)
                sp.dma_start(b2_sb[:, :], b2).then_inc(weights_in, 16)
                sp.dma_start(w3_sb[:, :], w3).then_inc(weights_in, 16)
                with sp.Fori(1, pairs) as r:
                    load_step(2 * r, 0, r)
                    load_step(2 * r + 1, 1, r)
                    load(2 * r, 0)
                    load(2 * r + 1, 1)
                sp.wait_ge(y_copied, tiles)
                sp.dma_start(out, y_row[0:1, :]).then_inc(y_out, 16)
                sp.wait_ge(y_out, 16)

            @block.gpsimd
            def _(pool):
                def gather(t, j, n):
                    if positive(t - 1):
                        pool.wait_ge(turned_act, len(ACT_GROUPS) * (t - 1))
                    pool.wait_ge(ids_in[j], 16 * n)
                    pool.sem_inc(gather_begun, 1)
                    for k in range(GATHERS):
                        nc.gpsimd.indirect_dma_start(
                            out=vecs[j][:, 1 + k, :], out_offset=None, in_=tables[k],
                            in_offset=bass.IndirectOffsetOnAxis(ap=ids_sb[j][:, k:k + 1], axis=0),
                        ).then_inc(gathered[j], 16)

                gather(0, 0, 1)
                gather(1, 1, 1)
                with pool.Fori(1, pairs) as r:
                    gather(2 * r, 0, r + 1)
                    gather(2 * r + 1, 1, r + 1)

            @block.tensor
            def _(pe):
                def turn_group(t, j, q):
                    if q in DVE_GROUPS:
                        n = len(DVE_GROUPS) * t + DVE_GROUPS.index(q)
                        bank, ready, copied, free = vec_dve, turned_dve, copied_dve, n
                    else:
                        k = ACT_GROUPS.index(q)
                        n = len(ACT_GROUPS) * t + k
                        bank, ready, copied, free = vec_act[(len(ACT_GROUPS) * j + k) % 2], turned_act, copied_act, n - 1
                    if positive(free):
                        pe.wait_ge(copied, free)
                    for v in range(q * GROUP, min(ROWS, (q + 1) * GROUP)):
                        last = nc.tensor.transpose(bank[:, v - q * GROUP, :], vecs[j][:, v, :], ident[:, :])
                    last.then_inc(ready, 1)

                def look_up(s, a, pair, i):
                    _, f, half = units(a)[i]
                    pe.wait_ge(onehot_made, LOOKUPS * s + i + 1)
                    if half == 0 and positive(LOOKUPS * pair + f):
                        pe.wait_ge(looked_up, LOOKUPS * pair + f)
                    for c in range(UNIT_CH):
                        ch = half * UNIT_CH + c
                        nc.tensor.matmul(look_ps, look_hi[:, f, ch, :], onehot[:, i, c, :],
                                         start=ch == 0, stop=False)
                        last = nc.tensor.matmul(look_ps, look_lo[:, f, ch, :], onehot[:, i, c, :],
                                                start=False, stop=ch == LOOK_CH - 1)
                    last.then_inc(onehot_used, 1)

                def pairs_out(t):
                    pe.wait_ge(folded, t + 1)
                    if positive(t):
                        pe.wait_ge(y_copied, t)
                    for c in range(CHUNKS):
                        last = nc.tensor.transpose(
                            pairs_ps[0:CHUNK, c, :],
                            pair_rows_sb[:, c * CHUNK:(c + 1) * CHUNK], ident[:, :])
                    last.then_inc(pairs_ready, 1)

                def layer1(t, j):
                    pe.wait_ge(pairs_copied, t + 1)
                    pe.wait_ge(dense_copied, t + 1)
                    if positive(t):
                        pe.wait_ge(h1_copied, t)
                    for o in range(H1 // P):
                        cols = slice(o * P, (o + 1) * P)
                        nc.tensor.matmul(hid1[:, o, :], w1d[:, 0, cols], dense_T[j][:, :], start=True, stop=False)
                        for c in range(CHUNKS):
                            k = CHUNK + 1 if c == 0 else CHUNK
                            last = nc.tensor.matmul(hid1[:, o, :], w1p[0:k, c, cols], pairs_T[0:k, c, :],
                                                    start=False, stop=c == CHUNKS - 1)
                    last.then_inc(h1_ready, 1)

                def layer2(t):
                    pe.wait_ge(h1_copied, t + 1)
                    for o in range(H2 // P):
                        for c in range(H1 // P):
                            last = nc.tensor.matmul(hid2[:, o, :], w2_sb[:, c, o * P:(o + 1) * P], h1_T[:, c, :],
                                                    start=c == 0, stop=c == H1 // P - 1)
                    last.then_inc(h2_ready, 1)

                def layer3(t):
                    pe.wait_ge(h2_copied, t + 1)
                    for c in range(H2 // P):
                        last = nc.tensor.matmul(y_ps, w3_sb[:, c:c + 1], h2_T[:, c, :],
                                                start=c == 0, stop=c == H2 // P - 1)
                    last.then_inc(y_ready, 1)

                def gram_part(j, part):
                    for g in range(GRAM_PARTS[part], GRAM_PARTS[part + 1]):
                        for s in range(P // QUAD):
                            v = vecs_T[j][:, s * QUAD + g, :]
                            last = nc.tensor.matmul(
                                gram[s * QUAD:s * QUAD + VECS, g, 0:2 * FOLD], v[:, 0:VECS],
                                v.rearrange("d (h n) -> d h n", h=2)[:, :, 0:FOLD], start=True, stop=True)
                    return last

                def tile(t, j, pair, mlp=True, look=True):
                    def unit(i):
                        if look and i < LOOKUPS:
                            look_up(t + 2, j, pair + 1, i)

                    pe.wait_ge(dense_in[j], 16 * (pair + 1))
                    pe.wait_ge(gathered[j], 16 * GATHERS * (pair + 1))
                    turn_group(t, j, 0)
                    turn_group(t, j, 1)
                    turn_group(t, j, 2)
                    if mlp:
                        pairs_out(t - 1)
                    turn_group(t, j, 3)
                    turn_group(t, j, 4)
                    if mlp:
                        layer1(t - 1, 1 - j)
                    unit(0)
                    if mlp:
                        layer2(t - 1)
                    unit(1)
                    pe.wait_ge(copied_dve, len(DVE_GROUPS) * (t + 1))
                    pe.wait_ge(copied_act, len(ACT_GROUPS) * (t + 1))
                    pe.wait_ge(merged, t + 1)
                    if positive(t):
                        pe.wait_ge(gram_turned, t)
                    gram_part(j, 0)
                    if mlp:
                        layer3(t - 1)
                    for part in range(1, len(GRAM_PARTS) - 1):
                        unit(part + 1)
                        last = gram_part(j, part)
                    last.then_inc(gram_ready, 1)

                pe.wait_ge(table_split, LOOKUPS)
                for s in range(2):
                    for i in range(LOOKUPS):
                        look_up(s, s, 0, i)
                pe.wait_ge(ident_in, 16)
                pe.wait_ge(dve_set, 3)
                tile(0, 0, 0, mlp=False)
                pe.wait_ge(weights_in, 6 * 16)
                pe.wait_ge(w1d_summed, 1)
                tile(1, 1, 0)
                with pe.Fori(1, pairs - 1) as r:
                    tile(2 * r, 0, r)
                    tile(2 * r + 1, 1, r)
                tile(tiles - 2, 0, pairs - 1, look=False)
                tile(tiles - 1, 1, pairs - 1, look=False)
                end = tiles - 1
                pairs_out(end)
                layer1(end, 1)
                layer2(end)
                layer3(end)

            def copy_group(engine_copy, bank, j, q):
                lo, hi = q * GROUP, min(ROWS, (q + 1) * GROUP)
                return engine_copy(vecs_T[j][:, :, lo:hi].rearrange("d b v -> d v b"), bank[:, 0:hi - lo, :])

            @block.vector
            def _(dve):
                def turn(t):
                    dve.wait_ge(gram_ready, t + 1)
                    nc.vector.transpose(gram_rows[:, :, :, :].rearrange("p h n m -> p (h n m)"),
                                        gram[:, :, 0:2 * FOLD].rearrange("p g n -> p n g")).then_inc(gram_turned, 1)
                    block_ip = pair_rows_sb[:, :].rearrange("p (i m) -> p i m", i=FOLD)
                    dve.wait_ge(gram_turned, t + 1)
                    if positive(t):
                        dve.wait_ge(pairs_ready, t)
                    nc.vector.tensor_copy(block_ip, gram_rows[:, 1, :, 0:VECS]).then_inc(half_copied, 1)
                    dve.wait_ge(half_copied, t + 1)
                    dve.sem_inc(fold_begun, 1)
                    nc.vector.copy_predicated(block_ip[:, :, HALF:VECS], mask[:, :, :],
                                              gram_rows[:, 0, :, 1:HALF]).then_inc(folded, 1)

                def copy(t, j, k):
                    dve.wait_ge(turned_dve, len(DVE_GROUPS) * t + k + 1)
                    copy_group(nc.vector.tensor_copy, vec_dve, j, DVE_GROUPS[k]).then_inc(copied_dve, 1)

                def make_onehot(s, a, n):
                    dve.wait_ge(step_ids_in[a], 16 * n)
                    for i, f, half in units(a):
                        if positive(s):
                            dve.wait_ge(onehot_used, LOOKUPS * (s - 1) + i + 1)
                        for c in range(UNIT_CH):
                            ch = half * UNIT_CH + c
                            last = nc.vector.tensor_scalar(
                                onehot[:, i, c, :], step_ids[a][0:LOOK_K, f - a * LOOKUPS // 2, :],
                                row_no[0:LOOK_K, ch:ch + 1], None, ALU.is_equal)
                        last.then_inc(onehot_made, 1)

                def tile(t, j, pair, turn_last=True, look=True):
                    if turn_last:
                        turn(t - 1)
                    copy(t, j, 0)
                    copy(t, j, 1)
                    if look:
                        make_onehot(t + 2, j, pair + 2)

                nc.vector.memset(gram[:, 0:16, :], 0.0).then_inc(dve_set, 1)
                nc.vector.memset(gram[:, 16:32, :], 0.0).then_inc(dve_set, 1)
                nc.vector.memset(pairs_T[96:P, :, :], 1.0).then_inc(dve_set, 1)
                dve.wait_ge(row_no_in, 16)
                make_onehot(0, 0, 1)
                for k in range(LOOKUPS):
                    dve.wait_ge(table_high, k + 1)
                    nc.vector.tensor_tensor(look_lo[:, k, :, :].rearrange("p c d -> p (c d)"), look_raw[k % 2][:, :],
                                            look_hi[:, k, :, :].rearrange("p c d -> p (c d)").bitcast(F32),
                                            ALU.subtract).then_inc(table_split, 1)
                make_onehot(1, 1, 1)
                tile(0, 0, 0, turn_last=False)
                dve.wait_ge(mask_in, 16)
                dve.wait_ge(weights_in, 6 * 16)
                nc.vector.tensor_tensor(w1d[:, 0, :], w1d[:, 0, :], w1d[:, 1, :], ALU.add).then_inc(w1d_summed, 1)
                tile(1, 1, 0)
                with dve.Fori(1, pairs - 1) as r:
                    tile(2 * r, 0, r)
                    tile(2 * r + 1, 1, r)
                tile(tiles - 2, 0, pairs - 1, look=False)
                tile(tiles - 1, 1, pairs - 1, look=False)
                turn(tiles - 1)

            @block.scalar
            def _(act):
                def copy(t, j, k):
                    bank = vec_act[(len(ACT_GROUPS) * j + k) % 2]
                    act.wait_ge(turned_act, len(ACT_GROUPS) * t + k + 1)
                    if k == 0:
                        nc.scalar.copy(dense_T[j][:, :], bank[:, 0, :]).then_inc(dense_copied, 1)
                    copy_group(nc.scalar.copy, bank, j, ACT_GROUPS[k]).then_inc(copied_act, 1)

                def pairs_in(t):
                    act.wait_ge(pairs_ready, t + 1)
                    nc.scalar.copy(pairs_T[0:CHUNK, :, :], pairs_ps[0:CHUNK, :, :]).then_inc(pairs_copied, 1)

                def relu1(t):
                    act.wait_ge(h1_ready, t + 1)
                    nc.scalar.activation(h1_T[:, :, :], hid1[:, :, :], ACT.Relu).then_inc(h1_copied, 1)

                def relu2(t):
                    act.wait_ge(h2_ready, t + 1)
                    nc.scalar.activation(h2_T[:, 0, :], hid2[:, 0, :], ACT.Relu, bias=b2_sb[:, 0:1])
                    nc.scalar.activation(h2_T[:, 1, :], hid2[:, 1, :], ACT.Relu,
                                         bias=b2_sb[:, 1:2]).then_inc(h2_copied, 1)

                def result(t):
                    act.wait_ge(y_ready, t + 1)
                    nc.scalar.copy(y_row[0:1, at(t)], y_ps).then_inc(y_copied, 1)

                def take_looked(s, a, pair, i):
                    _, f, half = units(a)[i]
                    if half == 1:
                        if f == 0 and positive(pair):
                            act.wait_ge(merged, 2 * pair)
                        act.wait_ge(onehot_used, LOOKUPS * s + i + 1)
                        nc.scalar.copy(looked[:, f, :], look_ps).then_inc(looked_up, 1)

                def merge(t, j, pair):
                    act.wait_ge(looked_up, LOOKUPS * (pair + 1))
                    nc.scalar.copy(vecs_T[j][:, :, ROWS:VECS].rearrange("d b v -> d v b"),
                                   looked[:, :, j * P:(j + 1) * P]).then_inc(merged, 1)

                def tile(t, j, pair, mlp=True, look=True):
                    def unit(i):
                        if look and i < LOOKUPS:
                            take_looked(t + 2, j, pair + 1, i)

                    copy(t, j, 0)
                    copy(t, j, 1)
                    if mlp:
                        pairs_in(t - 1)
                    copy(t, j, 2)
                    if j == 0:
                        merge(t, 0, pair)
                        merge(t + 1, 1, pair)
                    if mlp:
                        relu1(t - 1)
                    unit(0)
                    if mlp:
                        relu2(t - 1)
                    unit(1)
                    if mlp:
                        result(t - 1)
                    for i in range(2, LOOKUPS):
                        unit(i)

                for k in range(LOOKUPS):
                    act.wait_ge(table_in[k], 16)
                    nc.scalar.copy(look_hi[:, k, :, :].rearrange("p c d -> p (c d)"),
                                   look_raw[k % 2][:, :]).then_inc(table_high, 1)
                for s in range(2):
                    for i in range(LOOKUPS):
                        take_looked(s, s, 0, i)
                tile(0, 0, 0, mlp=False)
                act.wait_ge(dve_set, 3)
                act.wait_ge(weights_in, 6 * 16)
                tile(1, 1, 0)
                with act.Fori(1, pairs - 1) as r:
                    tile(2 * r, 0, r)
                    tile(2 * r + 1, 1, r)
                tile(tiles - 2, 0, pairs - 1, look=False)
                tile(tiles - 1, 1, pairs - 1, look=False)
                end = tiles - 1
                pairs_in(end)
                relu1(end)
                relu2(end)
                result(end)


def kernel(**inputs):
    import concourse.bacc as bacc
    from concourse.bass_utils import run_bass_kernel_spmd

    nc = bacc.Bacc("TRN2", target_bir_lowering=False, num_devices=1)
    w1 = np.asarray(inputs["W_top1"])
    dense = np.ascontiguousarray(inputs["r_dense_proj"])
    ids = np.asarray(inputs["ids"])
    small = [f for f in range(TABLES) if inputs[f"tbl_{f}"].shape[0] == LOOK_ROWS][:LOOKUPS]
    large = [f for f in range(TABLES) if f not in small]
    arrays = {
        "dense": dense,
        "ids": np.ascontiguousarray(ids[:, large]),
        "look_ids": np.ascontiguousarray(ids[:, small].T),
        "w1_dense": np.ascontiguousarray(np.concatenate([w1[0:D], w1[D + PAIRS:]], axis=0)),
        "w1_pairs": np.ascontiguousarray(w1[D:D + PAIRS][pair_rows(large + small)]),
        "b1": np.ascontiguousarray(np.asarray(inputs["b_top1"]).reshape(1, H1)),
        "w2": np.ascontiguousarray(inputs["W_top2"]),
        "b2": np.ascontiguousarray(np.asarray(inputs["b_top2"]).reshape(H2 // P, P).T),
        "w3": np.ascontiguousarray(np.asarray(inputs["W_top3"]).reshape(H2 // P, P).T),
        "fold_mask": np.ascontiguousarray(np.broadcast_to(
            np.triu(np.ones((FOLD, FOLD), np.int32)).reshape(1, -1), (P, FOLD * FOLD))),
        "identity": np.eye(P, dtype=np.float32),
        "row_numbers": np.arange(P * LOOK_CH, dtype=np.float32).reshape(P, LOOK_CH),
    }
    for f in range(TABLES):
        arrays[f"tbl_{f}"] = np.ascontiguousarray(inputs[f"tbl_{f}"])
    ap = {name: nc.dram_tensor(name, a.shape, mybir.dt.from_np(a.dtype), kind="ExternalInput").ap()
          for name, a in arrays.items()}
    out = nc.dram_tensor("y", (1, dense.shape[0]), F32, kind="ExternalOutput").ap()
    build(nc, ap["dense"], ap["ids"], ap["look_ids"], [ap[f"tbl_{f}"] for f in large],
          [ap[f"tbl_{f}"] for f in small], ap["w1_dense"], ap["w1_pairs"], ap["b1"], ap["w2"], ap["b2"],
          ap["w3"], ap["fold_mask"], ap["identity"], ap["row_numbers"], out)
    r = run_bass_kernel_spmd(nc, [arrays], core_ids=[0])
    return r.results[0]["y"].reshape(dense.shape[0], 1)
```

```python
from contextlib import ExitStack

import numpy as np

import concourse.bass as bass
from concourse import mybir

F32 = mybir.dt.float32
F32R = mybir.dt.float32r
I32 = mybir.dt.int32
ACT = mybir.ActivationFunctionType
ALU = mybir.AluOpType

P = 128
D = 128
TABLES = 26
VECS = TABLES + 1
LOOKUPS = 8
LOOK_ROWS = 1000
LOOK_K = 125
LOOK_CH = LOOK_ROWS // LOOK_K
UNIT_CH = LOOK_CH // 2
RAWS = 4
SLOTS = 4
GATHERS = TABLES - LOOKUPS
ROWS = 1 + GATHERS
ROW = 28
HALF = ROW // 2
FOLD = HALF - 1
QUAD = 32
PAIRS = VECS * (VECS - 1) // 2
CHUNKS = 3
CHUNK = PAIRS // CHUNKS
GROUP = 4
GROUPS = -(-ROWS // GROUP)
DVE_GROUPS = (2,)
ACT_GROUPS = (0, 1, 3, 4)
PARTS = LOOKUPS // 2
GRAM_PARTS = tuple(QUAD * n // PARTS for n in range(PARTS + 1))
H1, H2 = 512, 256


def pair_rows(fields):
    vector = [0] + [1 + f for f in fields]
    rows = []
    for i in range(FOLD):
        for p in range(VECS):
            a, b = (p, i + HALF) if p < i + HALF else (i, p - FOLD)
            a, b = sorted((vector[a], vector[b]))
            rows.append(a * VECS - a * (a + 1) // 2 + b - a - 1)
    return np.array(rows)


def build(nc, dense, ids, look_ids, tables, look_tables, w1_dense, w1_pairs, b1, w2, b2, w3,
          fold_mask, identity, row_numbers, out):
    batch = dense.shape[0]
    tiles = batch // P
    pairs = tiles // 2
    assert tiles % 2 == 0 and pairs >= 3 and len(tables) == GATHERS and GROUPS == 5
    PAIR = 2 * P

    with ExitStack() as ctx:
        def sb(name, shape, dt=F32):
            return ctx.enter_context(nc.sbuf_tensor(name, shape, dt))

        def psum(name, shape):
            return ctx.enter_context(nc.psum_tensor(name, shape, F32))

        def sem(name):
            return ctx.enter_context(nc.semaphore(name))

        ids_sb = [sb(f"ids{j}", [P, GATHERS], I32) for j in range(2)]
        vecs = [sb(f"vecs{j}", [P, ROWS, D]) for j in range(2)]
        vecs_T = [sb(f"vecs_T{j}", [D, P, ROW]) for j in range(2)]
        raw = [sb(f"raw{k}", [P, LOOK_CH * D]) for k in range(RAWS)]
        look_hi = sb("look_hi", [LOOK_K, LOOKUPS, LOOK_CH, D], F32R)
        look_lo = sb("look_lo", [LOOK_K, LOOKUPS, LOOK_CH, D], F32R)
        assert LOOKUPS % 2 == 0 and LOOKUPS % SLOTS == 0
        STEP_IDS = LOOKUPS // 2
        step_ids = [sb(f"step_ids{a}", [P, STEP_IDS, PAIR], I32) for a in range(2)]
        onehot = sb("onehot", [LOOK_K, SLOTS, UNIT_CH, PAIR], F32R)
        looked = sb("looked", [D, LOOKUPS, PAIR])
        row_no = sb("row_no", [P, LOOK_CH])
        gram_rows = sb("gram_rows", [P, 2, FOLD, QUAD])
        pair_rows_sb = sb("pair_rows_sb", [P, PAIRS])
        dense_hi, dense_lo = sb("dense_hi", [D, PAIR], F32R), sb("dense_lo", [D, PAIR], F32R)
        pairs_hi, pairs_lo = sb("pairs_hi", [P, CHUNKS, PAIR], F32R), sb("pairs_lo", [P, CHUNKS, PAIR], F32R)
        h1_hi, h1_lo = sb("h1_hi", [P, H1 // P, PAIR], F32R), sb("h1_lo", [P, H1 // P, PAIR], F32R)
        h2_T = raw[0][:, 0:H2 // P * PAIR].rearrange("p (c b) -> p c b", c=H2 // P)
        y_row = raw[1][0:1, 0:PAIR]
        w1_hi, w1_lo = sb("w1_hi", [P, 1 + CHUNKS, H1], F32R), sb("w1_lo", [P, 1 + CHUNKS, H1], F32R)
        w2_hi, w2_lo = sb("w2_hi", [P, H1 // P, H2], F32R), sb("w2_lo", [P, H1 // P, H2], F32R)
        b2_sb = sb("b2_sb", [P, H2 // P])
        w3_sb = sb("w3_sb", [P, H2 // P])
        ident = sb("ident", [P, P])
        mask = sb("mask", [P, FOLD, FOLD], I32)

        vec_dve = psum("vec_dve", [P, GROUP, P])
        vec_act = [psum(f"vec_act{j}", [P, GROUP, P]) for j in range(2)]
        gram = psum("gram", [P, QUAD, QUAD])
        small = psum("small", [P, 512])
        hid1 = psum("hid1", [P, 2, PAIR])
        look_bank = psum("look_ps", [D, 512])
        look_ps = look_bank[:, 0:PAIR]
        pairs_ps = small[:, 0:CHUNKS * P].rearrange("p (c b) -> p c b", c=CHUNKS)
        hid2 = small[:, :].rearrange("p (c b) -> p c b", c=H2 // P)
        y_ps = small[0:1, 0:PAIR]
        hid1_bank = hid1[:, :, :].rearrange("p o b -> p (o b)")
        pairs_end = [bank[:, 0:CHUNKS * P].rearrange("p (c b) -> p c b", c=CHUNKS) for bank in (look_bank, hid1_bank)]
        gram_banks = gram[:, :, :].rearrange("p g n -> p (g n)")
        vec_banks = [bank[:, :, :].rearrange("p v b -> p (v b)") for bank in (*vec_act, vec_dve)]
        hid1_end = [look_bank[:, 0:PAIR], gram_banks[:, 0:PAIR], gram_banks[:, 512:512 + PAIR], vec_banks[0][:, 0:PAIR]]
        hid2_end = [small[:, 0:PAIR], vec_banks[1][:, 0:PAIR]]
        y_end = vec_banks[2][0:1, 0:PAIR]

        W1_DENSE, W1_PAIRS01, W1_PAIRS2, W2 = range(LOOKUPS, LOOKUPS + 4)
        ITEMS = LOOKUPS + 4

        def parts(n):
            if n < LOOKUPS:
                return look_hi[:, n, :, :], look_lo[:, n, :, :]
            return {W1_DENSE: (w1_hi[:, 0:1, :], w1_lo[:, 0:1, :]),
                    W1_PAIRS01: (w1_hi[0:CHUNK, 1:3, :], w1_lo[0:CHUNK, 1:3, :]),
                    W1_PAIRS2: (w1_hi[0:CHUNK + 1, 3:4, :], w1_lo[0:CHUNK + 1, 3:4, :]),
                    W2: (w2_hi[:, :, :], w2_lo[:, :, :])}[n]

        def raw_as(n, k, chunks, width):
            return raw[n % RAWS][0:k, 0:chunks * width].rearrange("p (c n) -> p c n", c=chunks)

        def raw_part(n):
            return raw_as(n, *parts(n)[0].shape)

        ids_in = [sem(f"ids_in{j}") for j in range(2)]
        dense_in = [sem(f"dense_in{j}") for j in range(2)]
        gathered = [sem(f"gathered{j}") for j in range(2)]
        gathered_end = [sem(f"gathered_end{q}") for q in range(GROUPS)]
        step_ids_in = [sem(f"step_ids_in{a}") for a in range(2)]
        item_in = [sem(f"item_in{n}") for n in range(ITEMS)]
        item_high, item_split = sem("item_high"), sem("item_split")
        onehot_made, onehot_used, looked_up, merged = sem("onehot_made"), sem("onehot_used"), sem("looked_up"), sem("merged")
        gather_begun, fold_begun = sem("gather_begun"), sem("fold_begun")
        ident_in, weights_in, mask_in, row_no_in = sem("ident_in"), sem("weights_in"), sem("mask_in"), sem("row_no_in")
        dve_set, w1d_summed = sem("dve_set"), sem("w1d_summed")
        turned_dve, turned_act = sem("turned_dve"), sem("turned_act")
        copied_dve, copied_act = sem("copied_dve"), sem("copied_act")
        dense_high, dense_split = sem("dense_high"), sem("dense_split")
        gram_ready, gram_turned = sem("gram_ready"), sem("gram_turned")
        half_copied, folded = sem("half_copied"), sem("folded")
        pairs_ready, pairs_high, pairs_split = sem("pairs_ready"), sem("pairs_high"), sem("pairs_split")
        h1_ready, h1_high, h1_split = sem("h1_ready"), sem("h1_high"), sem("h1_split")
        h2_ready, h2_copied = sem("h2_ready"), sem("h2_copied")
        y_ready, y_copied, y_out = sem("y_ready"), sem("y_copied"), sem("y_out")

        def at(n):
            return bass.ds(n * P, P)

        def positive(n):
            return not isinstance(n, int) or n > 0

        FIRST_TURN = 4

        def units(a):
            return [(i, (a * LOOKUPS + i) // 2, (a * LOOKUPS + i) % 2) for i in range(LOOKUPS)]

        with nc.Block() as block:

            @block.sync
            def _(sp):
                def load_ids(t, j, n):
                    if positive(n):
                        sp.wait_ge(gathered[j], 16 * GATHERS * n)
                    sp.dma_start(ids_sb[j][:, :], ids[at(t), :]).then_inc(ids_in[j], 16)

                def load_dense(t, j):
                    if positive(t - 1):
                        sp.wait_ge(turned_act, len(ACT_GROUPS) * (t - 1))
                    sp.dma_start(vecs[j][:, 0, :], dense[at(t), :]).then_inc(dense_in[j], 16)

                def load_step(s, a, pair):
                    if positive(s - 1):
                        sp.wait_ge(onehot_made, LOOKUPS * (s - 1))
                    first = a * LOOKUPS // 2
                    src = look_ids[first:first + STEP_IDS, bass.ds(pair * PAIR, PAIR)]
                    sp.dma_start(step_ids[a][:, :, :],
                                 src.unsqueeze(0).broadcast_to([P, STEP_IDS, PAIR])).then_inc(step_ids_in[a], 16)

                def load_item(n, dst, src):
                    if n >= RAWS:
                        sp.wait_ge(item_split, n - RAWS + 1)
                    sp.dma_start(dst, src).then_inc(item_in[n], 16)

                def load_table(f):
                    load_item(f, raw_part(f), look_tables[f].rearrange("(p c) d -> p c d", c=LOOK_CH))

                load_ids(0, 0, 0)
                sp.dma_start(row_no[:, :], row_numbers).then_inc(row_no_in, 16)
                load_step(0, 0, 0)
                load_table(0)
                load_ids(1, 1, 0)
                sp.dma_start(ident[:, :], identity).then_inc(ident_in, 16)
                load_table(1)
                load_dense(0, 0)
                load_table(2)
                load_step(1, 1, 0)
                load_dense(1, 1)
                load_table(3)
                sp.dma_start(mask[:, :, :].rearrange("p i q -> p (i q)"), fold_mask).then_inc(mask_in, 16)
                sp.dma_start(b2_sb[:, :], b2).then_inc(weights_in, 16)
                sp.dma_start(w3_sb[:, :], w3).then_inc(weights_in, 16)
                for f in range(4, LOOKUPS):
                    load_table(f)
                load_item(W1_DENSE, raw_as(W1_DENSE, D, 2, H1), w1_dense.rearrange("(c k) n -> k c n", k=D))
                load_ids(2, 0, 1)
                load_step(2, 0, 1)
                load_item(W1_PAIRS01, raw_part(W1_PAIRS01),
                          w1_pairs[0:2 * CHUNK, :].rearrange("(c k) n -> k c n", k=CHUNK))
                load_dense(2, 0)
                load_item(W1_PAIRS2, raw_as(W1_PAIRS2, CHUNK, 1, H1)[:, 0, :], w1_pairs[2 * CHUNK:3 * CHUNK, :])
                load_item(W1_PAIRS2, raw_part(W1_PAIRS2)[CHUNK:CHUNK + 1, 0, :], b1)
                load_ids(3, 1, 1)
                load_step(3, 1, 1)
                load_item(W2, raw_part(W2), w2.rearrange("(c k) n -> k c n", k=P))
                load_dense(3, 1)
                with sp.Fori(2, pairs) as r:
                    load_ids(2 * r, 0, r)
                    load_step(2 * r, 0, r)
                    load_dense(2 * r, 0)
                    load_ids(2 * r + 1, 1, r)
                    load_step(2 * r + 1, 1, r)
                    load_dense(2 * r + 1, 1)
                sp.wait_ge(y_out, 16 * pairs)

            @block.gpsimd
            def _(pool):
                def gather(t, j, n, by_group=False):
                    if positive(t - 1):
                        pool.wait_ge(turned_act, len(ACT_GROUPS) * (t - 1))
                    pool.wait_ge(ids_in[j], 16 * n)
                    pool.sem_inc(gather_begun, 1)
                    for k in range(GATHERS):
                        nc.gpsimd.indirect_dma_start(
                            out=vecs[j][:, 1 + k, :], out_offset=None, in_=tables[k],
                            in_offset=bass.IndirectOffsetOnAxis(ap=ids_sb[j][:, k:k + 1], axis=0),
                        ).then_inc(gathered_end[(1 + k) // GROUP] if by_group else gathered[j], 16)

                gather(0, 0, 1)
                gather(1, 1, 1)
                with pool.Fori(1, pairs - 1) as r:
                    gather(2 * r, 0, r + 1)
                    gather(2 * r + 1, 1, r + 1)
                gather(tiles - 2, 0, pairs)
                gather(tiles - 1, 1, pairs, by_group=True)

            @block.tensor
            def _(pe):
                def turn_group(t, j, q):
                    if q in DVE_GROUPS:
                        n = len(DVE_GROUPS) * t + DVE_GROUPS.index(q)
                        bank, ready, copied, free = vec_dve, turned_dve, copied_dve, n
                    else:
                        k = ACT_GROUPS.index(q)
                        n = len(ACT_GROUPS) * t + k
                        bank, ready, copied, free = vec_act[k % 2], turned_act, copied_act, n - 1
                    if positive(free):
                        pe.wait_ge(copied, free)
                    for v in range(q * GROUP, min(ROWS, (q + 1) * GROUP)):
                        last = nc.tensor.transpose(bank[:, v - q * GROUP, :], vecs[j][:, v, :], ident[:, :])
                    last.then_inc(ready, 1)

                def look_up(s, a, pair, i):
                    _, f, half = units(a)[i]
                    if isinstance(pair, int) and pair == 0 and half == 0:
                        pe.wait_ge(item_split, f + 1)
                    pe.wait_ge(onehot_made, LOOKUPS * s + i + 1)
                    if half == 0 and positive(LOOKUPS * pair + f):
                        pe.wait_ge(looked_up, LOOKUPS * pair + f)
                    for c in range(UNIT_CH):
                        ch = half * UNIT_CH + c
                        nc.tensor.matmul(look_ps, look_hi[:, f, ch, :], onehot[:, i % SLOTS, c, :],
                                         start=ch == 0, stop=False)
                        last = nc.tensor.matmul(look_ps, look_lo[:, f, ch, :], onehot[:, i % SLOTS, c, :],
                                                start=False, stop=ch == LOOK_CH - 1)
                    last.then_inc(onehot_used, 1)

                def pairs_out(t, after=None, bank=pairs_ps):
                    pe.wait_ge(folded, t + 1)
                    if positive(t):
                        pe.wait_ge(pairs_split, t)
                    if after is not None:
                        pe.wait_ge(y_copied, after)
                    for c in range(CHUNKS):
                        last = nc.tensor.transpose(
                            bank[0:CHUNK, c, :],
                            pair_rows_sb[:, c * CHUNK:(c + 1) * CHUNK], ident[:, :])
                    last.then_inc(pairs_ready, 1)

                def product_parts(bank, w_hi, w_lo, x_hi, x_lo, k, k_lo, start, stop):
                    nc.tensor.matmul(bank, w_lo[0:k], x_hi[0:k], start=start, stop=False)
                    nc.tensor.matmul(bank, w_hi[0:k_lo], x_lo[0:k_lo], start=False, stop=False)
                    return nc.tensor.matmul(bank, w_hi[0:k], x_hi[0:k], start=False, stop=stop)

                def split_product(psum_out, operands):
                    for n, operand in enumerate(operands):
                        last = product_parts(psum_out, *operand, start=n == 0, stop=n == len(operands) - 1)
                    return last

                def layer1_operands(o):
                    cols = slice(o * P, (o + 1) * P)
                    operands = [(w1_hi[:, 0, cols], w1_lo[:, 0, cols], dense_hi[:, :], dense_lo[:, :], D, D)]
                    for c in range(CHUNKS):
                        k = CHUNK + (c == CHUNKS - 1)
                        operands.append((w1_hi[:, 1 + c, cols], w1_lo[:, 1 + c, cols],
                                         pairs_hi[:, c, :], pairs_lo[:, c, :], k, CHUNK))
                    return operands

                def layer2_operand(o, c):
                    cols = slice(o * P, (o + 1) * P)
                    return w2_hi[:, c, cols], w2_lo[:, c, cols], h1_hi[:, c, :], h1_lo[:, c, :], P, P

                def layer1(m, half):
                    if half == 0:
                        pe.wait_ge(pairs_split, 2 * m + 2)
                        pe.wait_ge(dense_split, 2 * m + 2)
                    if positive(2 * m + half):
                        pe.wait_ge(h1_split, 2 * m + half)
                    for o in range(2):
                        last = split_product(hid1[:, o, :], layer1_operands(2 * half + o))
                    last.then_inc(h1_ready, 1)

                def layer2(m, t):
                    pe.wait_ge(h1_split, 2 * m + 2)
                    pe.wait_ge(pairs_split, t)
                    for o in range(H2 // P):
                        last = split_product(hid2[:, o, :], [layer2_operand(o, c) for c in range(H1 // P)])
                    last.then_inc(h2_ready, 1)

                def layer3(m):
                    pe.wait_ge(h2_copied, m + 1)
                    for c in range(H2 // P):
                        last = nc.tensor.matmul(y_ps, w3_sb[:, c:c + 1], h2_T[:, c, :],
                                                start=c == 0, stop=c == H2 // P - 1)
                    last.then_inc(y_ready, 1)

                def gram_part(j, part):
                    for g in range(GRAM_PARTS[part], GRAM_PARTS[part + 1]):
                        for s in range(P // QUAD):
                            v = vecs_T[j][:, s * QUAD + g, :]
                            last = nc.tensor.matmul(
                                gram[s * QUAD:s * QUAD + VECS, g, 0:2 * FOLD], v[:, 0:VECS],
                                v.rearrange("d (h n) -> d h n", h=2)[:, :, 0:FOLD], start=True, stop=True)
                    return last

                def turn_rows(t, j, pair):
                    pe.wait_ge(dense_in[j], 16 * (pair + 1))
                    pe.wait_ge(gathered[j], 16 * GATHERS * (pair + 1))
                    for q in range(GROUPS):
                        turn_group(t, j, q)

                def wait_for_vecs(t):
                    pe.wait_ge(copied_dve, len(DVE_GROUPS) * (t + 1))
                    pe.wait_ge(copied_act, len(ACT_GROUPS) * (t + 1))
                    pe.wait_ge(merged, t + 1)
                    if positive(t):
                        pe.wait_ge(gram_turned, t)

                def tile(t, j, pair, first=False, mlp=True, look=True):
                    def unit(i):
                        if look:
                            look_up(t + 2, j, pair + 1, i)

                    if not first:
                        turn_rows(t, j, pair)
                        pairs_out(t - 1, after=pair - 1 if j == 0 and positive(pair - 1) else None)
                    unit(0)
                    unit(1)
                    if not look:
                        wait_for_vecs(t)
                        for part in range(PARTS):
                            last = gram_part(j, part)
                        last.then_inc(gram_ready, 1)
                        layer1(pair - 1, 0)
                        return
                    if mlp and j == 0:
                        layer1(pair - 1, 0)
                    if mlp and j == 1:
                        layer2(pair - 1, t)
                    wait_for_vecs(t)
                    gram_part(j, 0)
                    unit(2)
                    if mlp and j == 0:
                        layer1(pair - 1, 1)
                    if mlp and j == 1:
                        layer3(pair - 1)
                    unit(3)
                    for part in range(1, PARTS):
                        last = gram_part(j, part)
                        if part < PARTS - 1:
                            unit(2 * part + 2)
                            unit(2 * part + 3)
                    last.then_inc(gram_ready, 1)

                pe.wait_ge(ident_in, 16)
                pe.wait_ge(dve_set, 3)
                for i in range(LOOKUPS):
                    look_up(0, 0, 0, i)
                for i in range(LOOKUPS):
                    if i == FIRST_TURN:
                        turn_rows(0, 0, 0)
                    look_up(1, 1, 0, i)
                tile(0, 0, 0, first=True, mlp=False)
                tile(1, 1, 0, mlp=False)
                pe.wait_ge(item_split, ITEMS)
                pe.wait_ge(weights_in, 2 * 16)
                with pe.Fori(1, pairs - 1) as r:
                    tile(2 * r, 0, r)
                    tile(2 * r + 1, 1, r)
                tile(tiles - 2, 0, pairs - 1, look=False)
                last = tiles - 1
                pe.wait_ge(dense_in[1], 16 * pairs)
                for q in range(GROUPS):
                    if q == 3:
                        pairs_out(last - 1, bank=pairs_end[0])
                        layer1(pairs - 2, 1)
                    first, end = max(1, q * GROUP), min(ROWS, (q + 1) * GROUP)
                    pe.wait_ge(gathered_end[q], 16 * (end - first))
                    turn_group(last, 1, q)
                wait_for_vecs(last)
                for part in range(PARTS):
                    end = gram_part(1, part)
                end.then_inc(gram_ready, 1)
                layer2(pairs - 2, last - 1)
                pairs_out(last, bank=pairs_end[1])
                pe.wait_ge(dense_split, tiles)
                pe.wait_ge(gram_turned, tiles)
                pe.wait_ge(pairs_split, last)
                end_ops = [layer1_operands(o) for o in range(H1 // P)]
                for o in range(H1 // P):
                    product_parts(hid1_end[o], *end_ops[o][0], start=True, stop=False)
                layer3(pairs - 2)
                pe.wait_ge(pairs_split, tiles)
                for o in range(H1 // P):
                    for c in range(1, 1 + CHUNKS):
                        end = product_parts(hid1_end[o], *end_ops[o][c], start=False, stop=c == CHUNKS)
                    end.then_inc(h1_ready, 1)
                pe.wait_ge(y_copied, pairs - 1)
                for c in range(H1 // P):
                    pe.wait_ge(h1_split, 2 * (pairs - 1) + c + 1)
                    for o in range(H2 // P):
                        end = product_parts(hid2_end[o], *layer2_operand(o, c), start=c == 0, stop=c == H1 // P - 1)
                        if c == H1 // P - 1:
                            end.then_inc(h2_ready, 1)
                for c in range(H2 // P):
                    pe.wait_ge(h2_copied, pairs - 1 + c + 1)
                    end = nc.tensor.matmul(y_end, w3_sb[:, c:c + 1], h2_T[:, c, :],
                                           start=c == 0, stop=c == H2 // P - 1)
                end.then_inc(y_ready, 1)

            def copy_group(engine_copy, bank, j, q):
                lo, hi = q * GROUP, min(ROWS, (q + 1) * GROUP)
                return engine_copy(vecs_T[j][:, :, lo:hi].rearrange("d b v -> d v b"), bank[:, 0:hi - lo, :])

            @block.vector
            def _(dve):
                def turn(t):
                    dve.wait_ge(gram_ready, t + 1)
                    nc.vector.transpose(gram_rows[:, :, :, :].rearrange("p h n m -> p (h n m)"),
                                        gram[:, :, 0:2 * FOLD].rearrange("p g n -> p n g")).then_inc(gram_turned, 1)
                    block_ip = pair_rows_sb[:, :].rearrange("p (i m) -> p i m", i=FOLD)
                    dve.wait_ge(gram_turned, t + 1)
                    if positive(t):
                        dve.wait_ge(pairs_ready, t)
                    nc.vector.tensor_copy(block_ip, gram_rows[:, 1, :, 0:VECS]).then_inc(half_copied, 1)
                    dve.wait_ge(half_copied, t + 1)
                    dve.sem_inc(fold_begun, 1)
                    nc.vector.copy_predicated(block_ip[:, :, HALF:VECS], mask[:, :, :],
                                              gram_rows[:, 0, :, 1:HALF]).then_inc(folded, 1)

                def copy(t, j, k):
                    dve.wait_ge(turned_dve, len(DVE_GROUPS) * t + k + 1)
                    copy_group(nc.vector.tensor_copy, vec_dve, j, DVE_GROUPS[k]).then_inc(copied_dve, 1)

                def make_unit(s, a, i, f, half):
                    if positive(LOOKUPS * s + i + 1 - SLOTS):
                        dve.wait_ge(onehot_used, LOOKUPS * s + i + 1 - SLOTS)
                    for c in range(UNIT_CH):
                        ch = half * UNIT_CH + c
                        last = nc.vector.tensor_scalar(
                            onehot[:, i % SLOTS, c, :], step_ids[a][0:LOOK_K, f - a * LOOKUPS // 2, :],
                            row_no[0:LOOK_K, ch:ch + 1], None, ALU.is_equal)
                    last.then_inc(onehot_made, 1)

                def take_low(n):
                    dve.wait_ge(item_high, n + 1)
                    hi, lo = parts(n)
                    nc.vector.tensor_tensor(lo, raw_part(n), hi.bitcast(F32), ALU.subtract).then_inc(item_split, 1)

                def pairs_low(t, j, bank=pairs_ps):
                    dve.wait_ge(pairs_high, t + 1)
                    at_t = slice(j * P, (j + 1) * P)
                    nc.vector.tensor_tensor(pairs_lo[0:CHUNK, :, at_t], bank[0:CHUNK, :, :],
                                            pairs_hi[0:CHUNK, :, at_t].bitcast(F32), ALU.subtract).then_inc(pairs_split, 1)

                def dense_low(t, j):
                    dve.wait_ge(dense_high, t + 1)
                    at_t = slice(j * P, (j + 1) * P)
                    nc.vector.tensor_tensor(dense_lo[:, at_t], vecs_T[j][:, :, 0],
                                            dense_hi[:, at_t].bitcast(F32), ALU.subtract).then_inc(dense_split, 1)

                def h1_low(m, half):
                    dve.wait_ge(h1_high, 2 * m + half + 1)
                    outs = slice(2 * half, 2 * half + 2)
                    nc.vector.scalar_tensor_tensor(out=h1_lo[:, outs, :], in0=hid1[:, :, :], scalar=0.0,
                                                   in1=h1_hi[:, outs, :].bitcast(F32), op0=ALU.max,
                                                   op1=ALU.subtract).then_inc(h1_split, 1)

                def tile(t, j, pair, first=False, mlp=True, look=True, items=()):
                    made = units(j)

                    def unit(i):
                        if look:
                            make_unit(t + 2, j, *made[i])

                    if look:
                        dve.wait_ge(step_ids_in[j], 16 * (pair + 2))
                    unit(0)
                    unit(1)
                    if not first:
                        turn(t - 1)
                        copy(t, j, 0)
                        pairs_low(t - 1, 1 - j)
                    unit(2)
                    if j == 1:
                        dense_low(t - 1, 0)
                        dense_low(t, 1)
                    if mlp and j == 0 and look:
                        h1_low(pair - 1, 0)
                    unit(3)
                    unit(4)
                    if mlp and j == 0 and look:
                        h1_low(pair - 1, 1)
                    for i in range(5, LOOKUPS):
                        unit(i)
                    for n in items:
                        take_low(n)

                nc.vector.memset(gram[:, 0:16, :], 0.0).then_inc(dve_set, 1)
                nc.vector.memset(gram[:, 16:32, :], 0.0).then_inc(dve_set, 1)
                nc.vector.memset(pairs_hi[96:P, CHUNKS - 1, :].bitcast(F32), 1.0).then_inc(dve_set, 1)
                dve.wait_ge(row_no_in, 16)
                for s in range(2):
                    dve.wait_ge(step_ids_in[s], 16)
                    for i, f, half in units(s):
                        if s == 1 and i == FIRST_TURN + 2:
                            copy(0, 0, 0)
                        make_unit(s, s, i, f, half)
                        if half == 1:
                            take_low(f)
                dve.wait_ge(item_in[W1_DENSE], 16)
                both = raw_as(W1_DENSE, D, 2, H1)
                nc.vector.tensor_tensor(both[:, 0, :], both[:, 0, :], both[:, 1, :], ALU.add).then_inc(w1d_summed, 1)
                tile(0, 0, 0, first=True, mlp=False, items=(W1_DENSE, W1_PAIRS01))
                dve.wait_ge(mask_in, 16)
                tile(1, 1, 0, mlp=False, items=(W1_PAIRS2, W2))
                with dve.Fori(1, pairs - 1) as r:
                    tile(2 * r, 0, r)
                    tile(2 * r + 1, 1, r)
                tile(tiles - 2, 0, pairs - 1, look=False)
                last = tiles - 1
                turn(last - 1)
                h1_low(pairs - 2, 0)
                copy(last, 1, 0)
                h1_low(pairs - 2, 1)
                pairs_low(last - 1, 0, pairs_end[0])
                dense_low(last - 1, 0)
                dense_low(last, 1)
                turn(last)
                pairs_low(last, 1, pairs_end[1])
                for o in range(H1 // P):
                    dve.wait_ge(h1_high, 2 * (pairs - 1) + o + 1)
                    nc.vector.scalar_tensor_tensor(out=h1_lo[:, o, :], in0=hid1_end[o], scalar=0.0,
                                                   in1=h1_hi[:, o, :].bitcast(F32), op0=ALU.max,
                                                   op1=ALU.subtract).then_inc(h1_split, 1)

            @block.scalar
            def _(act):
                def copy(t, j, k):
                    bank = vec_act[k % 2]
                    act.wait_ge(turned_act, len(ACT_GROUPS) * t + k + 1)
                    if k == 0 and positive(t - 1):
                        act.wait_ge(dense_split, t - 1)
                    copy_group(nc.scalar.copy, bank, j, ACT_GROUPS[k]).then_inc(copied_act, 1)

                def dense_to_high(t, j, copied):
                    act.wait_ge(copied_act, copied)
                    nc.scalar.copy(dense_hi[:, j * P:(j + 1) * P], vecs_T[j][:, :, 0]).then_inc(dense_high, 1)

                def pairs_to_high(t, j, bank=pairs_ps):
                    act.wait_ge(pairs_ready, t + 1)
                    nc.scalar.copy(pairs_hi[0:CHUNK, :, j * P:(j + 1) * P], bank[0:CHUNK, :, :]).then_inc(pairs_high, 1)

                def relu1(m, half):
                    act.wait_ge(h1_ready, 2 * m + half + 1)
                    nc.scalar.activation(h1_hi[:, 2 * half:2 * half + 2, :], hid1[:, :, :], ACT.Relu).then_inc(h1_high, 1)

                def relu2(m):
                    act.wait_ge(h2_ready, m + 1)
                    nc.scalar.activation(h2_T[:, 0, :], hid2[:, 0, :], ACT.Relu, bias=b2_sb[:, 0:1])
                    nc.scalar.activation(h2_T[:, 1, :], hid2[:, 1, :], ACT.Relu,
                                         bias=b2_sb[:, 1:2]).then_inc(h2_copied, 1)

                def result(m, bank=y_ps):
                    act.wait_ge(y_ready, m + 1)
                    if positive(m):
                        act.wait_ge(y_out, 16 * m)
                    nc.scalar.copy(y_row, bank).then_inc(y_copied, 1)
                    act.wait_ge(y_copied, m + 1)
                    act.dma_start(out[0:1, bass.ds(m * PAIR, PAIR)], y_row).then_inc(y_out, 16)

                def take_looked(s, a, pair, i):
                    _, f, half = units(a)[i]
                    if half == 1:
                        if f == 0 and positive(pair):
                            act.wait_ge(merged, 2 * pair)
                        act.wait_ge(onehot_used, LOOKUPS * s + i + 1)
                        nc.scalar.copy(looked[:, f, :], look_ps).then_inc(looked_up, 1)

                def merge(t, j, pair):
                    act.wait_ge(looked_up, LOOKUPS * (pair + 1))
                    nc.scalar.copy(vecs_T[j][:, :, ROWS:VECS].rearrange("d b v -> d v b"),
                                   looked[:, :, j * P:(j + 1) * P]).then_inc(merged, 1)

                def copies(t, j):
                    for k in range(len(ACT_GROUPS)):
                        copy(t, j, k)

                def dense_pair(pair):
                    dense_to_high(2 * pair, 0, len(ACT_GROUPS) * 2 * pair + 1)
                    dense_to_high(2 * pair + 1, 1, len(ACT_GROUPS) * (2 * pair + 1) + 1)

                def tile(t, j, pair, first=False, mlp=True, look=True, items=()):
                    def unit(i):
                        if look:
                            take_looked(t + 2, j, pair + 1, i)

                    if j == 0:
                        merge(t, 0, pair)
                    if not first:
                        copies(t, j)
                        pairs_to_high(t - 1, 1 - j)
                    unit(0)
                    if j == 0:
                        merge(t + 1, 1, pair)
                        unit(1)
                        if mlp:
                            relu1(pair - 1, 0)
                    else:
                        unit(1)
                        dense_pair(pair)
                        if mlp:
                            relu2(pair - 1)
                    unit(2)
                    if mlp and j == 0 and look:
                        relu1(pair - 1, 1)
                    if mlp and j == 1:
                        result(pair - 1)
                    unit(3)
                    for n in items:
                        take_high(n)
                    for i in range(4, LOOKUPS):
                        unit(i)

                def take_high(n):
                    act.wait_ge(item_in[n], 16 * (2 if n == W1_PAIRS2 else 1))
                    nc.scalar.copy(parts(n)[0], raw_part(n)).then_inc(item_high, 1)

                ahead = LOOKUPS // 2
                for k in range(ahead):
                    take_high(k)
                for s in range(2):
                    for i, f, half in units(s):
                        if s == 1 and i == FIRST_TURN:
                            copies(0, 0)
                        take_looked(s, s, 0, i)
                        if half == 1 and f + ahead < LOOKUPS:
                            take_high(f + ahead)
                act.wait_ge(w1d_summed, 1)
                tile(0, 0, 0, first=True, mlp=False, items=(W1_DENSE, W1_PAIRS01))
                act.wait_ge(dve_set, 3)
                act.wait_ge(weights_in, 2 * 16)
                tile(1, 1, 0, mlp=False, items=(W1_PAIRS2, W2))
                with act.Fori(1, pairs - 1) as r:
                    tile(2 * r, 0, r)
                    tile(2 * r + 1, 1, r)
                tile(tiles - 2, 0, pairs - 1, look=False)
                last = tiles - 1
                copy(last, 1, 0)
                copy(last, 1, 1)
                relu1(pairs - 2, 1)
                copy(last, 1, 2)
                copy(last, 1, 3)
                pairs_to_high(last - 1, 0, pairs_end[0])
                dense_pair(pairs - 1)
                relu2(pairs - 2)
                pairs_to_high(last, 1, pairs_end[1])
                result(pairs - 2)
                for o in range(H1 // P):
                    act.wait_ge(h1_ready, 2 * (pairs - 1) + o + 1)
                    nc.scalar.activation(h1_hi[:, o, :], hid1_end[o], ACT.Relu).then_inc(h1_high, 1)
                for o in range(H2 // P):
                    act.wait_ge(h2_ready, pairs - 1 + o + 1)
                    nc.scalar.activation(h2_T[:, o, :], hid2_end[o], ACT.Relu, bias=b2_sb[:, o:o + 1]).then_inc(h2_copied, 1)
                result(pairs - 1, y_end)


def kernel(**inputs):
    import concourse.bacc as bacc
    from concourse.bass_utils import run_bass_kernel_spmd

    nc = bacc.Bacc("TRN2", target_bir_lowering=False, num_devices=1)
    w1 = np.asarray(inputs["W_top1"])
    dense = np.ascontiguousarray(inputs["r_dense_proj"])
    ids = np.asarray(inputs["ids"])
    small = [f for f in range(TABLES) if inputs[f"tbl_{f}"].shape[0] == LOOK_ROWS][:LOOKUPS]
    large = [f for f in range(TABLES) if f not in small]
    arrays = {
        "dense": dense,
        "ids": np.ascontiguousarray(ids[:, large]),
        "look_ids": np.ascontiguousarray(ids[:, small].T),
        "w1_dense": np.ascontiguousarray(np.concatenate([w1[0:D], w1[D + PAIRS:]], axis=0)),
        "w1_pairs": np.ascontiguousarray(w1[D:D + PAIRS][pair_rows(large + small)]),
        "b1": np.ascontiguousarray(np.asarray(inputs["b_top1"]).reshape(1, H1)),
        "w2": np.ascontiguousarray(inputs["W_top2"]),
        "b2": np.ascontiguousarray(np.asarray(inputs["b_top2"]).reshape(H2 // P, P).T),
        "w3": np.ascontiguousarray(np.asarray(inputs["W_top3"]).reshape(H2 // P, P).T),
        "fold_mask": np.ascontiguousarray(np.broadcast_to(
            np.triu(np.ones((FOLD, FOLD), np.int32)).reshape(1, -1), (P, FOLD * FOLD))),
        "identity": np.eye(P, dtype=np.float32),
        "row_numbers": np.arange(P * LOOK_CH, dtype=np.float32).reshape(P, LOOK_CH),
    }
    for f in range(TABLES):
        arrays[f"tbl_{f}"] = np.ascontiguousarray(inputs[f"tbl_{f}"])
    ap = {name: nc.dram_tensor(name, a.shape, mybir.dt.from_np(a.dtype), kind="ExternalInput").ap()
          for name, a in arrays.items()}
    out = nc.dram_tensor("y", (1, dense.shape[0]), F32, kind="ExternalOutput").ap()
    build(nc, ap["dense"], ap["ids"], ap["look_ids"], [ap[f"tbl_{f}"] for f in large],
          [ap[f"tbl_{f}"] for f in small], ap["w1_dense"], ap["w1_pairs"], ap["b1"], ap["w2"], ap["b2"],
          ap["w3"], ap["fold_mask"], ap["identity"], ap["row_numbers"], out)
    r = run_bass_kernel_spmd(nc, [arrays], core_ids=[0])
    return r.results[0]["y"].reshape(dense.shape[0], 1)
```
